# Optimizing a Trainium2 kernel written in Bass

```python
import numpy as np
import jax
import jax.numpy as jnp

def _softmax(x, axis=-1):
    return jax.nn.softmax(x, axis=axis)

def _gelu(x):
    return jax.nn.gelu(x, approximate=True)

def _silu(x):
    return jax.nn.silu(x)

def _sigmoid(x):
    return jax.nn.sigmoid(x)

def _layernorm(x, axis=-1, eps=1e-05):
    m = jnp.mean(x, axis=axis, keepdims=True)
    v = jnp.var(x, axis=axis, keepdims=True)
    return (x - m) / jnp.sqrt(v + eps)

def _scatter_add(tgt, idx, src, axis=0):
    return tgt.at[idx].add(src)

def _segment_sum(src, seg, n):
    return jax.ops.segment_sum(src, seg, n)
kernel_name = 'mk_gnn_preln_d1_gnn_r16_1d33c8'

def setup_inputs(seed: int=0):
    np.random.seed(seed)
    _w = jnp.asarray

    def _rec_inputs():
        import jax
        import jax.numpy as jnp
        _gk = jax.random.key(seed)
        x = -4.079e-06 + 0.02 * jax.random.normal(jax.random.fold_in(_gk, 1), (6250, 128), jnp.float32)
        _s = jax.random.randint(jax.random.fold_in(_gk, 2), (50000,), 0, 6250, jnp.int32)
        _d = jax.random.randint(jax.random.fold_in(_gk, 3), (50000,), 0, 6250, jnp.int32)
        _loop = jnp.arange(6250, dtype=jnp.int32)
        src = jnp.concatenate([_s, _d, _loop])
        dst = jnp.concatenate([_d, _s, _loop])
        _o = jnp.argsort(dst, stable=True)
        src = src[_o]
        dst = dst[_o]
        return (x, src, dst)
    x, src, dst = _rec_inputs()

    def _L0_gnn_setup():
        import jax, jax.numpy as jnp
        import numpy as np
        N_NODES = 3125
        D = 128
        N_EDGES = 50000

        def _gcn_conv(x, src, dst, ew, W, b, n):
            h = x @ W
            loop = jnp.arange(n)
            s = jnp.concatenate([src, loop])
            d = jnp.concatenate([dst, loop])
            w = jnp.concatenate([ew, jnp.ones((n,), x.dtype)])
            deg = jax.ops.segment_sum(w, d, num_segments=n)
            dinv = jnp.where(deg > 0, jax.lax.rsqrt(deg), 0.0)
            norm = dinv[s] * w * dinv[d]
            out = jax.ops.segment_sum(h[s] * norm[:, None], d, num_segments=n)
            return out + b

        def _edge_encoder(x, src, dst, We, be):
            H = x.shape[-1]
            logits = x[src] @ We[:H] + x[dst] @ We[H:] + be
            return jax.nn.sigmoid(logits[:, 0])

        def _node_encoder(x, src, dst, ev, Wn, bn, n):
            agg = jax.ops.segment_sum(ev[:, None] * x[src], dst, num_segments=n)
            return jax.nn.relu(agg @ Wn + bn)
        key = jax.random.key(seed)
        ks = jax.random.split(key, 8)
        emb = jax.random.normal(ks[0], (N_NODES, D), jnp.float32) * 0.02
        emb = emb.at[0].set(0.0)
        edge_index = jax.random.randint(ks[1], (2, N_EDGES), 0, N_NODES, dtype=jnp.int64)
        W1 = jax.random.normal(ks[2], (D, 2 * D), jnp.float32) / np.sqrt(D)
        b1 = jnp.zeros((2 * D,), jnp.float32)
        We1 = jax.random.normal(ks[3], (4 * D, 1), jnp.float32) / np.sqrt(4 * D)
        be1 = jnp.zeros((1,), jnp.float32)
        Wn1 = jax.random.normal(ks[4], (2 * D, 2 * D), jnp.float32) / np.sqrt(2 * D)
        bn1 = jnp.zeros((2 * D,), jnp.float32)
        We2 = jax.random.normal(ks[5], (4 * D, 1), jnp.float32) / np.sqrt(4 * D)
        be2 = jnp.zeros((1,), jnp.float32)
        W2 = jax.random.normal(ks[6], (2 * D, D), jnp.float32) / np.sqrt(2 * D)
        b2 = jnp.zeros((D,), jnp.float32)
        return {'embedding': emb, 'edge_index': edge_index, 'W1': W1, 'b1': b1, 'We1': We1, 'be1': be1, 'Wn1': Wn1, 'bn1': bn1, 'We2': We2, 'be2': be2, 'W2': W2, 'b2': b2}
    _L0_gnn_all = _L0_gnn_setup()
    _L0_gnn_in = {k: v for k, v in _L0_gnn_all.items() if k in ('W1', 'b1', 'We1', 'be1', 'Wn1', 'bn1', 'We2', 'be2', 'W2', 'b2')}
    del _L0_gnn_all
    return {'x': x, 'src': src, 'dst': dst, 'L0_gnn_W1': _L0_gnn_in['W1'], 'L0_gnn_b1': _L0_gnn_in['b1'], 'L0_gnn_We1': _L0_gnn_in['We1'], 'L0_gnn_be1': _L0_gnn_in['be1'], 'L0_gnn_Wn1': _L0_gnn_in['Wn1'], 'L0_gnn_bn1': _L0_gnn_in['bn1'], 'L0_gnn_We2': _L0_gnn_in['We2'], 'L0_gnn_be2': _L0_gnn_in['be2'], 'L0_gnn_W2': _L0_gnn_in['W2'], 'L0_gnn_b2': _L0_gnn_in['b2']}

def reference(x, src, dst, L0_gnn_W1, L0_gnn_b1, L0_gnn_We1, L0_gnn_be1, L0_gnn_Wn1, L0_gnn_bn1, L0_gnn_We2, L0_gnn_be2, L0_gnn_W2, L0_gnn_b2):
    import jax
    import jax.numpy as jnp

    def _L0_gnn_ref(embedding, edge_index, W1, b1, We1, be1, Wn1, bn1, We2, be2, W2, b2):
        import jax, jax.numpy as jnp
        import numpy as np
        N_NODES = 3125
        D = 128
        N_EDGES = 50000

        def _gcn_conv(x, src, dst, ew, W, b, n):
            h = x @ W
            loop = jnp.arange(n)
            s = jnp.concatenate([src, loop])
            d = jnp.concatenate([dst, loop])
            w = jnp.concatenate([ew, jnp.ones((n,), x.dtype)])
            deg = jax.ops.segment_sum(w, d, num_segments=n)
            dinv = jnp.where(deg > 0, jax.lax.rsqrt(deg), 0.0)
            norm = dinv[s] * w * dinv[d]
            out = jax.ops.segment_sum(h[s] * norm[:, None], d, num_segments=n)
            return out + b

        def _edge_encoder(x, src, dst, We, be):
            H = x.shape[-1]
            logits = x[src] @ We[:H] + x[dst] @ We[H:] + be
            return jax.nn.sigmoid(logits[:, 0])

        def _node_encoder(x, src, dst, ev, Wn, bn, n):
            agg = jax.ops.segment_sum(ev[:, None] * x[src], dst, num_segments=n)
            return jax.nn.relu(agg @ Wn + bn)
        n = embedding.shape[0]
        src, dst = (edge_index[0], edge_index[1])
        ones_e = jnp.ones((src.shape[0],), embedding.dtype)
        h = _gcn_conv(embedding, src, dst, ones_e, W1, b1, n)
        nrm = jnp.sqrt(jnp.sum(h * h, axis=-1, keepdims=True))
        h = h / jnp.maximum(nrm, 1e-12)
        ev = _edge_encoder(h, src, dst, We1, be1)
        na = _node_encoder(h, src, dst, ev, Wn1, bn1, n)
        ev2 = _edge_encoder(na, src, dst, We2, be2)
        g = _node_encoder(na, src, dst, ev2, Wn1, bn1, n)
        out = _gcn_conv(g, src, dst, ev2, W2, b2, n)
        return out
    edge_index = jnp.stack([src, dst])
    h = jnp.maximum(_layernorm(x, axis=-1), 0.0)
    x = x + _L0_gnn_ref(h, edge_index, L0_gnn_W1, L0_gnn_b1, L0_gnn_We1, L0_gnn_be1, L0_gnn_Wn1, L0_gnn_bn1, L0_gnn_We2, L0_gnn_be2, L0_gnn_W2, L0_gnn_b2)
    return x

_drawn_inputs = setup_inputs


def setup_inputs(seed=0):
    import zlib

    import numpy as np

    out = dict(_drawn_inputs(seed))
    spreads = {'L0_gnn_b1': (0.0, 0.1), 'L0_gnn_bn1': (0.0, 0.1), 'L0_gnn_b2': (0.0, 0.1)}
    factors = {'L0_gnn_We1': 5.77}
    for name, (base, spread) in spreads.items():
        noise = np.random.default_rng([zlib.crc32(name.encode()), seed]).standard_normal(out[name].shape)
        drawn = base * np.exp(spread * noise) if base else spread * noise
        out[name] = jnp.asarray(drawn.astype(out[name].dtype))
    for name, factor in factors.items():
        out[name] = (out[name] * factor).astype(out[name].dtype)
    return out
```

```python
from contextlib import ExitStack

import concourse.bass as bass
from concourse import mybir

PART = 128
NODES, FEAT = 6250, 128
HID = 2 * FEAT
EDGES = 106250
NODE_TILES = -(-NODES // PART)
LAST_ROWS = NODES - (NODE_TILES - 1) * PART
NODES_PAD = NODE_TILES * PART
EDGE_TILES = -(-EDGES // PART)
PAIRS = EDGE_TILES - 1 + NODE_TILES
UNROLL = 16
TURNS = -(-PAIRS // UNROLL)
PAIRS = TURNS * UNROLL
BLOCKS = -(-max(PAIRS, EDGE_TILES + 1) // PART)
TABLE = BLOCKS * PART
DEG_TURNS = -(-EDGE_TILES // UNROLL)
SPARE = NODE_TILES
PAD_DST = SPARE * PART
GROUP = 7
NODE_TURNS = NODE_TILES // GROUP
SHIFT = PART.bit_length() - 1
W_RING = 4
EXT = HID + 2 + FEAT
ROW2, ROW3 = FEAT + 4, HID + 4
ACC3 = HID + 2
LN_EPS, NORM_EPS = 1e-05, 1e-12


def gnn_kernel(nc, x, src, dst, W1, b1, We1, be1, Wn1, bn1, We2, be2, W2, b2,
               ident_in, iota_in, pair_no_in, tile_no_in, out):
    fp32, bf16, i32, u32 = mybir.dt.float32, mybir.dt.bfloat16, mybir.dt.int32, mybir.dt.uint32
    ALU = mybir.AluOpType
    ACT = mybir.ActivationFunctionType
    AX = mybir.AxisListType
    VEC, SCA = mybir.EngineType.DVE, mybir.EngineType.Activation

    ctx = ExitStack()
    with ctx:
        def sb(name, shape, dt=fp32):
            return ctx.enter_context(nc.sbuf_tensor(name, shape, dt))

        def sem(name):
            return ctx.enter_context(nc.semaphore(name))

        tables = [nc.dram_tensor(f"table{k + 1}", [NODES_PAD, w], fp32).ap()
                  for k, w in enumerate((FEAT, ROW2, ROW3, FEAT))]
        widths = (FEAT, ROW2, ROW3, FEAT)

        ident = sb("ident", [PART, PART])
        iota = sb("iota", [PART, PART])
        iota16 = sb("iota16", [PART, PART], bf16)
        pair_no = sb("pair_no", [PART, BLOCKS])
        tile_no = sb("tile_no", [1, TABLE])
        ones = sb("ones", [PART, PART])
        w1e = sb("w1e", [PART, EXT])
        w1T = sb("w1T", [PART, 2, PART])
        w1n = sb("w1n", [PART, HID])
        wn1 = sb("wn1", [PART, 2, HID])
        w2 = sb("w2", [PART, 2, FEAT])
        we1 = sb("we1", [PART, 2, 2])
        we2_bc = sb("we2_bc", [PART, 2, HID])
        b1_bc = sb("b1_bc", [PART, HID + 2])
        b1n_bc = sb("b1n_bc", [PART, HID])
        b1_col = sb("b1_col", [PART, 2])
        b1_rep = sb("b1_rep", [PART, 2, PART])
        bn1_row = sb("bn1_row", [1, HID])
        bn1_col = sb("bn1_col", [PART, 2])
        b2_bc = sb("b2_bc", [PART, FEAT])
        be = sb("be", [PART, 2])

        dst_first = sb("dst_first", [1, TABLE], i32)
        entry = sb("entry", [1, TABLE])
        dst_low = sb("dst_low", [PART, TABLE])
        dst_high = sb("dst_high", [PART, TABLE], bf16)
        zeros16 = sb("zeros16", [PART, PART], bf16)
        tile_of = sb("tile_of", [PART, BLOCKS])
        tile_idx = sb("tile_idx", [PART, BLOCKS], u32)
        node_of = sb("node_of", [PART, BLOCKS])
        node_base = sb("node_base", [PART, BLOCKS])
        node_rows = sb("node_rows", [BLOCKS, PART], i32)
        node_row = sb("node_row", [1, TABLE], i32)
        pair_src = sb("pair_src", [PART, TABLE], u32)
        pair_dst = sb("pair_dst", [PART, TABLE])
        gate_ring = sb("gate_ring", [PART, UNROLL])
        gate2 = sb("gate2", [PART, TABLE])

        xbuf = sb("xbuf", [PART, NODE_TILES + 1, FEAT])
        low = sb("low", [PART, (NODE_TILES + 1) * ACC3])
        high = sb("high", [PART, NODE_TILES * ROW3])
        acc1 = low[:, 0:(NODE_TILES + 1) * FEAT].rearrange("p (j f) -> p j f", f=FEAT)
        acc2 = low[:, (NODE_TILES + 1) * FEAT + 2:][:, 0:(NODE_TILES + 1) * (FEAT + 1)].rearrange(
            "p (j f) -> p j f", f=FEAT + 1)
        acc3 = low[:, :].rearrange("p (j f) -> p j f", f=ACC3)
        acc4 = high[:, 0:(NODE_TILES + 1) * FEAT].rearrange("p (j f) -> p j f", f=FEAT)
        squares = high[:, FEAT * NODE_TILES:2 * FEAT * NODE_TILES].rearrange("p (j f) -> p j f", f=FEAT)
        tab1 = high[:, 0:NODE_TILES * FEAT].rearrange("p (j f) -> p j f", f=FEAT)
        tab2 = high[:, 0:NODE_TILES * ROW2].rearrange("p (j f) -> p j f", f=ROW2)
        tab3 = high[:, :].rearrange("p (j f) -> p j f", f=ROW3)
        tab4 = acc4[:, 0:NODE_TILES, :]
        xn = xbuf[:, 0:NODE_TILES, :]
        stat = sb("stat", [PART, 4, NODE_TILES])
        dinv = sb("dinv", [PART, NODE_TILES])
        dinv2 = sb("dinv2", [PART, NODE_TILES])
        att = sb("att", [PART, NODE_TILES, 2])
        norm_sq = sb("norm_sq", [PART, NODE_TILES])
        rnorm = sb("rnorm", [PART, NODE_TILES])
        row_scale = sb("row_scale", [PART, NODE_TILES])
        gate_dst = sb("gate_dst", [PART, NODE_TILES])
        diag = sb("diag", [PART, GROUP, PART])
        scrap = sb("scrap", [PART, 2, HID])
        scores = sb("scores", [PART, GROUP, 2])
        credit = sb("credit", [PART, 11])
        gate_open = sb("gate_open", [PART, 2])
        idx_ring = sb("idx_ring", [PART, UNROLL], u32)
        rows = sb("rows", [PART, UNROLL, ROW3])
        gates = sb("gates", [PART, W_RING, PART])
        weights = sb("weights", [PART, W_RING, PART])

        def within(whole, at, shape, dt=fp32):
            size = 1
            for n in shape:
                size *= n
            words = size if dt in (fp32, i32) else size // 2
            part = whole[:, at:at + words]
            part = part if dt == fp32 else part.bitcast(dt)
            names = "abc"[:len(shape)]
            return part.rearrange(f"p ({' '.join(names)}) -> p {' '.join(names)}", **dict(zip(names, shape))) if len(shape) > 1 else part

        setup = low[:, (NODE_TILES + 1) * FEAT:]
        edge_rows = within(setup, 0, [BLOCKS, PART], i32)
        edge_int = within(setup, TABLE, [2, BLOCKS, PART], i32)
        edge_f32 = within(setup, 3 * TABLE, [2, BLOCKS, PART])
        entry_bc = within(setup, 5 * TABLE, [TABLE])
        between = rows[:, :, :].rearrange("p a b -> p (a b)")
        low_hot = within(between, TABLE, [UNROLL, PART], bf16)
        high_hot = within(between, TABLE + UNROLL * PART // 2, [2, UNROLL, NODE_TILES + 1], bf16)
        hbuf = within(between, 0, [GROUP, HID])
        staged_acc = within(between, GROUP * HID, [GROUP, PART])
        gT = within(between, 0, [2, GROUP * PART])

        ps = [ctx.enter_context(nc.psum_tensor(f"ps{i}", [PART, 512], fp32)) for i in range(8)]

        ld_edges, ld_first, ld_const, ld_wa, ld_wb = (sem(n) for n in ("ld_edges", "ld_first", "ld_const", "ld_wa", "ld_wb"))
        ld_x, ld_x_last, ld_x2 = sem("ld_x"), sem("ld_x_last"), sem("ld_x2")
        const_ready = sem("const_ready")
        x_pad = sem("x_pad")
        dve_chain, act_chain = sem("dve_chain"), sem("act_chain")
        entry_ready, entry_sent = sem("entry_ready"), sem("entry_sent")
        halves_ready = sem("halves_ready")
        setup_block, setup_moved = sem("setup_block"), sem("setup_moved")
        pair_tiles_ready = sem("pair_tiles_ready")
        got_src, got_dst = ([sem(f"got_{n}{k}") for k in range(BLOCKS)] for n in ("src", "dst"))
        pair_parts_ready = sem("pair_parts_ready")
        node_of_sent, node_rows_ready, ld_node_row = sem("node_of_sent"), sem("node_rows_ready"), sem("ld_node_row")
        high_ready, low_ready, tiles_counted = sem("high_ready"), sem("low_ready"), sem("tiles_counted")
        deg_ready, sqrt_need, sqrt_done = sem("deg_ready"), sem("sqrt_need"), sem("sqrt_done")
        centred, squared = sem("centred"), sem("squared")
        tab_ready, tab_stored = sem("tab_ready"), [sem(f"tab_stored{k}") for k in range(4)]
        w1T_sent, w1T_ready, b1_rep_ready, w_prod, w_prod_ready = (
            sem(n) for n in ("w1T_sent", "w1T_ready", "b1_rep_ready", "w_prod", "w_prod_ready"))
        idx_staged, half_begun = sem("idx_staged"), sem("half_begun")
        landed = [sem(f"landed{u}") for u in range(UNROLL)]
        weights_ready, gates_ready, gates_kept = sem("weights_ready"), sem("gates_ready"), sem("gates_kept")
        pairs_done, pairs_added = sem("pairs_done"), sem("pairs_added")
        tiles_staged, tiles_done = sem("tiles_staged"), sem("tiles_done")
        psum_read, u_moved, h_ready, h_squared = sem("psum_read"), sem("u_moved"), sem("h_ready"), sem("h_squared")
        acc_cleared = sem("acc_cleared")
        diag_ready, bc_sent, bc_moved = sem("diag_ready"), sem("bc_sent"), sem("bc_moved")
        pre_ready, act3_ready, scored, rows3_ready = sem("pre_ready"), sem("act3_ready"), sem("scored"), sem("rows3_ready")
        g_sent, g_moved, hw_sent, hw_scaled = sem("g_sent"), sem("g_moved"), sem("hw_sent"), sem("hw_scaled")
        xb_ready, fin_ready, stored = sem("xb_ready"), sem("fin_ready"), sem("stored")

        def node_view(t):
            return t.rearrange("(j p) f -> p j f", p=PART)

        block = ctx.enter_context(nc.Block())

        @block.sync
        def _(sp):
            with nc.allow_non_contiguous_dma("first destination of each edge tile"):
                sp.dma_start(dst_first[:, :], dst[:, 0:1].rearrange("t o -> o t")).then_inc(ld_first, 16)
            sp.dma_start(edge_rows[:, :, :], dst.rearrange("(k q) e -> q k e", q=PART)).then_inc(ld_edges, 16)
            sp.dma_start(xbuf[:, 0:NODE_TILES - 1, :], node_view(x[0:(NODE_TILES - 1) * PART, :])).then_inc(ld_x, 16)
            sp.wait_ge(x_pad, 1)
            sp.dma_start(xbuf[0:LAST_ROWS, NODE_TILES - 1, :], x[(NODE_TILES - 1) * PART:NODES, :]).then_inc(ld_x_last, 16)
            sp.wait_ge(node_rows_ready, 1)
            sp.dma_start(node_row[0:1, :], node_rows[:, :]).then_inc(ld_node_row, 16)

            def store(k, tab, turn_of):
                for i in range(NODE_TURNS):
                    sp.wait_ge(tab_ready, turn_of + i + 1)
                    sp.dma_start(node_view(tables[k])[:, GROUP * i:GROUP * (i + 1), :],
                                 tab[:, GROUP * i:GROUP * (i + 1), :]).then_inc(tab_stored[k], 16)

            store(0, tab1, 0)
            store(1, tab2, NODE_TURNS)
            store(2, tab3, 2 * NODE_TURNS)
            sp.wait_ge(pairs_added, W_RING + 3 * PAIRS)
            sp.dma_start(xbuf[:, 0:NODE_TILES - 1, :], node_view(x[0:(NODE_TILES - 1) * PART, :])).then_inc(ld_x2, 16)
            sp.dma_start(xbuf[0:LAST_ROWS, NODE_TILES - 1, :], x[(NODE_TILES - 1) * PART:NODES, :]).then_inc(ld_x2, 16)
            store(3, tab4, 3 * NODE_TURNS)
            for i in range(NODE_TURNS):
                sp.wait_ge(fin_ready, i + 1)
                full = GROUP * (i + 1) if i < NODE_TURNS - 1 else NODE_TILES - 1
                sp.dma_start(node_view(out[0:(NODE_TILES - 1) * PART, :])[:, GROUP * i:full, :],
                             acc4[:, GROUP * i:full, :]).then_inc(stored, 16)
            sp.dma_start(out[(NODE_TILES - 1) * PART:NODES, :], acc4[0:LAST_ROWS, NODE_TILES - 1, :]).then_inc(stored, 16)
            sp.wait_ge(stored, 16 * (NODE_TURNS + 1))

        @block.gpsimd
        def _(pool):
            nc.gpsimd.memset(credit[:, 0:1], 0.0).then_inc(pairs_done, UNROLL)
            nc.gpsimd.memset(credit[:, 1:2], 0.0).then_inc(pairs_added, W_RING)
            nc.gpsimd.memset(credit[:, 2:3], 0.0).then_inc(tiles_done, GROUP)
            nc.gpsimd.memset(credit[:, 3:4], 0.0).then_inc(psum_read, GROUP)
            nc.gpsimd.memset(credit[:, 4:5], 0.0).then_inc(u_moved, GROUP)
            nc.gpsimd.memset(credit[:, 5:6], 0.0).then_inc(h_squared, GROUP)
            nc.gpsimd.memset(credit[:, 6:7], 0.0).then_inc(pre_ready, GROUP)
            nc.gpsimd.memset(credit[:, 7:8], 0.0).then_inc(rows3_ready, GROUP)
            nc.gpsimd.memset(credit[:, 9:10], 0.0).then_inc(hw_sent, 2)
            nc.gpsimd.memset(credit[:, 10:11], 0.0).then_inc(hw_scaled, 2)
            nc.gpsimd.memset(credit[:, 8:9], 0.0).then_inc(tiles_counted, 2 * UNROLL)
            pool.wait_ge(pair_tiles_ready, 1)
            pool.wait_ge(setup_moved, 4)
            for k in range(BLOCKS):
                index = bass.IndirectOffsetOnAxis(ap=tile_idx[:, k:k + 1], axis=0)
                nc.gpsimd.indirect_dma_start(edge_int[:, 0, k, :], None, src, index).then_inc(got_src[k], 16)
                nc.gpsimd.indirect_dma_start(edge_int[:, 1, k, :], None, dst, index).then_inc(got_dst[k], 16)
            def gather_pass(k):
                pool.wait_ge(tab_stored[k], 16 * NODE_TURNS)
                with pool.Fori(0, TURNS) as i:
                    for h in range(2):
                        pool.wait_ge(idx_staged, i * 2 + (2 * (TURNS + 1) * k + 1 + h))
                        nc.gpsimd.tensor_tensor(gate_open[:, h:h + 1], credit[:, 0:1], credit[:, 0:1], ALU.add).then_inc(half_begun, 1)
                        for u in range(h * UNROLL // 2, (h + 1) * UNROLL // 2):
                            nc.gpsimd.indirect_dma_start(
                                rows[:, u, 0:widths[k]], None, tables[k],
                                bass.IndirectOffsetOnAxis(ap=idx_ring[:, u:u + 1], axis=0)).then_inc(landed[u], 16)

            gather_pass(0)
            pool.wait_ge(pairs_added, W_RING + PAIRS)
            with pool.Fori(0, NODE_TURNS) as i:
                for u in range(GROUP):
                    pool.wait_ge(tiles_done, i * GROUP + (u + 1))
                    nc.gpsimd.tensor_copy(staged_acc[:, u, :].unsqueeze(1), acc1[:, bass.ds(i * GROUP + u, 1), :]).then_inc(tiles_staged, 1)
            gather_pass(1)
            pool.wait_ge(pairs_added, W_RING + 2 * PAIRS)
            pool.wait_ge(tab_stored[1], 16 * NODE_TURNS)
            with pool.Fori(0, NODE_TURNS) as i:
                def keep(u):
                    pool.wait_ge(act3_ready, i * GROUP + (u + 1))
                    nc.gpsimd.tensor_copy(tab3[:, bass.ds(i * GROUP + u, 1), 0:HID], hbuf[:, u, :].unsqueeze(1)).then_inc(rows3_ready, 1)

                for u in range(GROUP):
                    pool.wait_ge(tiles_done, i * GROUP + (NODE_TILES + u + 1))
                    nc.gpsimd.tensor_copy(staged_acc[:, u, :].unsqueeze(1), acc2[:, bass.ds(i * GROUP + u, 1), 0:FEAT]).then_inc(tiles_staged, 1)
                    if u > 1:
                        keep(u - 2)
                keep(GROUP - 2)
                keep(GROUP - 1)
            gather_pass(2)
            gather_pass(3)

        @block.scalar
        def _(act):
            act.dma_start(ident[:, :], ident_in).then_inc(ld_const, 16)
            act.dma_start(iota[:, :], iota_in).then_inc(ld_const, 16)
            act.dma_start(pair_no[:, :], pair_no_in).then_inc(ld_const, 16)
            act.dma_start(tile_no[:, :], tile_no_in).then_inc(ld_const, 16)
            act.dma_start(w1e[:, 0:HID], W1).then_inc(ld_wa, 16)
            act.dma_start(w1e[:, HID + 2:EXT], ident_in).then_inc(ld_wa, 16)
            act.dma_start(wn1[:, :, :], Wn1.rearrange("(c p) n -> p c n", p=PART)).then_inc(ld_wa, 16)
            with nc.allow_non_contiguous_dma("columns of weights and biases"):
                act.dma_start(we1[:, :, 0], We1[0:HID, 0].rearrange("(c p) -> p c", p=PART)).then_inc(ld_wa, 16)
                act.dma_start(we1[:, :, 1], We1[HID:2 * HID, 0].rearrange("(c p) -> p c", p=PART)).then_inc(ld_wa, 16)
                act.dma_start(b1_col[:, :], b1.rearrange("(c p) -> p c", p=PART)).then_inc(ld_wa, 16)
                act.dma_start(bn1_col[:, :], bn1.rearrange("(c p) -> p c", p=PART)).then_inc(ld_wb, 16)
            act.dma_start(b1_bc[:, 0:HID], b1.partition_broadcast(PART)).then_inc(ld_wb, 16)
            act.dma_start(bn1_row[:, :], bn1.rearrange("(o n) -> o n", o=1)).then_inc(ld_wb, 16)
            act.dma_start(w2[:, :, :], W2.rearrange("(c p) n -> p c n", p=PART)).then_inc(ld_wb, 16)
            act.dma_start(we2_bc[:, :, :], We2.rearrange("(c n) o -> c (n o)", c=2).partition_broadcast(PART)).then_inc(ld_wb, 16)
            act.dma_start(b2_bc[:, :], b2.partition_broadcast(PART)).then_inc(ld_wb, 16)
            act.dma_start(be[:, 0:1], be1.partition_broadcast(PART)).then_inc(ld_wb, 16)
            act.dma_start(be[:, 1:2], be2.partition_broadcast(PART)).then_inc(ld_wb, 16)

            def moved(r, dst_ap, cols):
                act.wait_ge(setup_block, r + 1)
                act.activation(dst_ap, ps[4 + r % 4][:, 0:cols], ACT.Copy).then_inc(setup_moved, 1)

            for c, part in enumerate((dst_low, dst_high)):
                moved(2 * c, part[:, 0:512], 512)
                moved(2 * c + 1, part[:, 512:TABLE], TABLE - 512)
            act.wait_ge(w1T_sent, 1)
            act.activation(w1T[:, :, :], ps[3][:, 0:HID].rearrange("p (c n) -> p c n", c=2), ACT.Copy).then_inc(w1T_ready, 1)
            act.wait_ge(centred, 1)
            act.activation(squares, xn, ACT.Square).then_inc(squared, 1)
            act.wait_ge(w_prod, 1)
            act.activation(w1e[:, HID:HID + 2], ps[3][:, 0:2], ACT.Copy).then_inc(w_prod_ready, 1)
            act.activation(w1n[:, :], ps[3][:, 2:2 + HID], ACT.Copy).then_inc(w_prod_ready, 1)
            act.wait_ge(w_prod, 2)
            act.activation(b1_bc[:, HID:HID + 2], ps[0][:, 0:2], ACT.Copy).then_inc(w_prod_ready, 1)
            act.activation(b1n_bc[:, :], ps[0][:, 2:2 + HID], ACT.Copy).then_inc(w_prod_ready, 1)
            moved(4, pair_src[:, 0:512], 512)
            moved(5, pair_src[:, 512:TABLE], TABLE - 512)
            moved(6, pair_dst[:, 0:512], 512)
            moved(7, pair_dst[:, 512:TABLE], TABLE - 512)

            def root(n, dst_ap, src_ap):
                act.wait_ge(sqrt_need, n)
                act.activation(dst_ap, src_ap, ACT.Sqrt).then_inc(sqrt_done, 1)

            root(1, stat[:, 2, :], stat[:, 1, :])
            root(2, dinv[:, :], stat[:, 3, :])
            for r in range(-(-NODE_TILES // 4)):
                n = min(4, NODE_TILES - 4 * r)
                act.wait_ge(setup_block, 8 + r + 1)
                act.activation(acc1[:, 4 * r:4 * r + n, :].rearrange("p j f -> p (j f)"),
                               ps[4 + r % 4][:, 0:n * PART], ACT.Copy).then_inc(setup_moved, 1)

            with act.Fori(0, NODE_TURNS) as i:
                for u in range(GROUP):
                    j = i * GROUP + u
                    act.wait_ge(tiles_done, j + (GROUP + 1))
                    act.activation(tab2[:, bass.ds(j, 1), 0:FEAT].rearrange("p o f -> p (o f)"),
                                   ps[u][:, HID + 2:EXT], ACT.Copy).then_inc(u_moved, 1)
                    act.wait_ge(h_ready, j + 1)
                    act.activation(hbuf[:, u, :], hbuf[:, u, :], ACT.Square,
                                   accum_out=norm_sq[:, bass.ds(j, 1)]).then_inc(h_squared, 1)
            root(3, rnorm[:, :], norm_sq[:, :])

            def gate_rows(phase):
                for i in range(NODE_TURNS):
                    for h, (lo, n) in enumerate(((0, 4), (4, GROUP - 4))):
                        t = 2 * (NODE_TURNS * phase + i) + h
                        act.wait_ge(bc_sent, t + 1)
                        act.activation(xbuf[:, GROUP * i + lo:GROUP * i + lo + n, :].rearrange("p j f -> p (j f)"),
                                       ps[4 + t % 4][:, 0:n * PART], ACT.Copy).then_inc(bc_moved, 1)

            def gate_pass(k):
                source_term = FEAT + 1 if k == 1 else HID
                act.wait_ge(ld_node_row, 16)
                with act.Fori(0, TURNS) as i:
                    _, nodes = nc.values_load_multi_w_load_instructions(
                        node_row[0:1, bass.ds(i * UNROLL, UNROLL)], engines=[SCA], min_val=0, max_val=SPARE,
                        skip_runtime_bounds_check_because="the staircase has no more node tiles")
                    for u in range(UNROLL):
                        n = i * UNROLL + (PAIRS * k + u)
                        act.wait_ge(landed[u], i * 16 + 16 * (TURNS * k + 1))
                        act.wait_ge(weights_ready, n + (1 - W_RING))
                        act.activation(gates[:, u % W_RING, :], xbuf[:, bass.ds(nodes[u], 1), :].rearrange("p o f -> p (o f)"),
                                       ACT.Sigmoid, bias=rows[:, u, source_term:source_term + 1]).then_inc(gates_ready, 1)

            gate_rows(0)
            gate_pass(1)
            with act.Fori(0, NODE_TURNS) as i:
                for u in range(GROUP):
                    j = i * GROUP + u
                    act.wait_ge(pre_ready, j + (GROUP + 1))
                    act.activation(hbuf[:, u, :], hbuf[:, u, :], ACT.Relu).then_inc(act3_ready, 1)
            gate_rows(1)
            gate_pass(2)
            root(4, dinv2[:, :], stat[:, 0, :])
            with act.Fori(0, NODE_TURNS) as i:
                act.wait_ge(hw_sent, i * 2 + 2)
                for m in range(2):
                    for h, (lo, n) in enumerate(((0, 4), (4, GROUP - 4))):
                        act.wait_ge(g_sent, i * 4 + (2 * m + h + 1))
                        act.activation(gT[:, m, lo * PART:(lo + n) * PART], ps[2 * m + h][:, 0:n * PART],
                                       ACT.Relu, bias=bn1_col[:, m:m + 1]).then_inc(g_moved, 1)

        @block.tensor
        def _(pe):
            def transposed(r, blocks):
                if r >= 4:
                    pe.wait_ge(setup_moved, r - 3)
                for c, blk in enumerate(blocks):
                    last = nc.tensor.transpose(ps[4 + r % 4][:, c * PART:(c + 1) * PART], blk, ident[:, :])
                last.then_inc(setup_block, 1)

            pe.wait_ge(ld_const, 64)
            pe.wait_ge(const_ready, 1)
            pe.wait_ge(entry_ready, 1)
            for h in range(2):
                last = nc.tensor.matmul(ps[h][:, 0:TABLE // 2], ones[0:1, :], entry[:, h * (TABLE // 2):(h + 1) * (TABLE // 2)],
                                        start=True, stop=True)
            last.then_inc(entry_sent, 1)
            pe.wait_ge(halves_ready, 1)
            for c in range(2):
                transposed(2 * c, [edge_f32[:, c, k, :] for k in range(4)])
                transposed(2 * c + 1, [edge_f32[:, c, k, :] for k in range(4, BLOCKS)])
            pe.wait_ge(ld_wa, 96)
            for c in range(2):
                last = nc.tensor.transpose(ps[3][:, c * PART:(c + 1) * PART], w1e[:, c * PART:(c + 1) * PART], ident[:, :])
            last.then_inc(w1T_sent, 1)
            pe.wait_ge(w1T_ready, 1)
            pe.wait_ge(b1_rep_ready, 2)
            pe.wait_ge(pair_tiles_ready, 1)
            for bank, left in ((3, w1T), (0, b1_rep)):
                for at, right in ((0, we1), (2, wn1)):
                    n = right.shape[2]
                    for c in range(2):
                        last = nc.tensor.matmul(ps[bank][:, at:at + n], left[:, c, :], right[:, c, :],
                                                start=(c == 0), stop=(c == 1), skip_group_check=True)
                last.then_inc(w_prod, 1)
            nc.tensor.transpose(ps[1][0:BLOCKS, 0:PART], node_of[:, :], ident[:, :]).then_inc(node_of_sent, 1)
            nc.tensor.matmul(ps[2][:, 0:NODE_TILES + 1], zeros16[:, :], zeros16[:, 0:NODE_TILES + 1], start=True, stop=False, skip_group_check=True)
            with pe.Fori(0, DEG_TURNS // 2) as i:
                for h in range(2):
                    pe.wait_ge(high_ready, i * 2 + (h + 1))
                    for u in range(UNROLL):
                        pe.wait_ge(low_ready, i * (2 * UNROLL) + (h * UNROLL + u + 1))
                        nc.tensor.matmul(ps[2][:, 0:NODE_TILES + 1], low_hot[:, u, :], high_hot[:, h, u, :],
                                         start=False, stop=False, skip_group_check=True).then_inc(tiles_counted, 1)
            nc.tensor.matmul(ps[2][:, 0:NODE_TILES + 1], zeros16[:, :], zeros16[:, 0:NODE_TILES + 1],
                             start=False, stop=True, skip_group_check=True).then_inc(deg_ready, 1)
            for c in range(2):
                pe.wait_ge(pair_parts_ready, c + 1)
                transposed(4 + 2 * c, [edge_f32[:, c, k, :] for k in range(4)])
                transposed(5 + 2 * c, [edge_f32[:, c, k, :] for k in range(4, BLOCKS)])
            pe.wait_ge(tab_ready, NODE_TURNS)
            for r in range(-(-NODE_TILES // 4)):
                transposed(8 + r, [tab1[:, j, :] for j in range(4 * r, min(4 * r + 4, NODE_TILES))])

            def multiply_pass(k):
                with pe.Fori(0, TURNS) as i:
                    for u in range(UNROLL):
                        n = i * UNROLL + (PAIRS * k + u)
                        bank, w, g = ps[u % W_RING], weights[:, u % W_RING, :], rows[:, u, :]
                        pe.wait_ge(weights_ready, n + 1)
                        pe.wait_ge(landed[u], i * 16 + 16 * (TURNS * k + 1))
                        pe.wait_ge(pairs_added, n + 1)
                        if k == 0:
                            last = nc.tensor.matmul(bank[:, 0:PART], g[:, 0:FEAT], w, start=True, stop=True)
                        elif k == 1:
                            nc.tensor.matmul(bank[:, 0:PART], g[:, 0:FEAT], w, start=True, stop=True, skip_group_check=True)
                            last = nc.tensor.matmul(bank[:, PART:PART + 1], w, g[:, FEAT:FEAT + 1], start=True, stop=True, skip_group_check=True)
                        elif k == 2:
                            for c in range(2):
                                nc.tensor.matmul(bank[:, c * PART:(c + 1) * PART], g[:, c * FEAT:(c + 1) * FEAT], w,
                                                 start=True, stop=True, skip_group_check=True)
                            last = nc.tensor.matmul(bank[:, HID:HID + 1], w, ones[:, 0:1], start=True, stop=True, skip_group_check=True)
                        else:
                            last = nc.tensor.matmul(bank[:, 0:FEAT], w, g[:, 0:FEAT], start=True, stop=True)
                        last.then_inc(pairs_done, 1)

            def broadcast_gates(phase):
                for i in range(NODE_TURNS):
                    pe.wait_ge(diag_ready, NODE_TURNS * phase + i + 1)
                    for h, (lo, n) in enumerate(((0, 4), (4, GROUP - 4))):
                        t = 2 * (NODE_TURNS * phase + i) + h
                        if t >= 4:
                            pe.wait_ge(bc_moved, t - 3)
                        nc.tensor.matmul(ps[4 + t % 4][:, 0:n * PART], ones[:, :],
                                         diag[:, lo:lo + n, :].rearrange("p j f -> p (j f)"), start=True, stop=True).then_inc(bc_sent, 1)

            pe.wait_ge(w_prod_ready, 4)
            pe.wait_ge(ld_wb, 128)
            multiply_pass(0)
            with pe.Fori(0, NODE_TURNS) as i:
                for u in range(GROUP):
                    j = i * GROUP + u
                    pe.wait_ge(tiles_staged, j + 1)
                    pe.wait_ge(psum_read, j + 1)
                    pe.wait_ge(u_moved, j + 1)
                    nc.tensor.matmul(ps[u][:, 0:EXT], staged_acc[:, u, :], w1e[:, :], start=True, stop=True).then_inc(tiles_done, 1)
            broadcast_gates(0)
            multiply_pass(1)
            with pe.Fori(0, NODE_TURNS) as i:
                for u in range(GROUP):
                    m = i * GROUP + (NODE_TILES + u)
                    pe.wait_ge(tiles_staged, m + 1)
                    pe.wait_ge(pre_ready, i * GROUP + (u + 1))
                    nc.tensor.matmul(ps[u][:, 0:HID], staged_acc[:, u, :], w1n[:, :], start=True, stop=False)
                    nc.tensor.matmul(ps[u][:, 0:HID], ones[0:1, :], bn1_row[:, :], start=False, stop=True).then_inc(tiles_done, 1)
            broadcast_gates(1)
            multiply_pass(2)
            pe.wait_ge(pairs_added, W_RING + 3 * PAIRS)
            with pe.Fori(0, NODE_TURNS) as i:
                for m in range(2):
                    for h, (lo, n) in enumerate(((0, 4), (4, GROUP - 4))):
                        for c in range(2):
                            last = nc.tensor.matmul(ps[2 * m + h][:, 0:n * PART].rearrange("p (j f) -> p j f", f=PART),
                                                    wn1[:, c, m * PART:(m + 1) * PART],
                                                    acc3[:, bass.ds(i * GROUP + lo, n), c * PART:(c + 1) * PART],
                                                    start=(c == 0), stop=(c == 1))
                        last.then_inc(g_sent, 1)
                pe.wait_ge(g_moved, i * 4 + 4)
                for h, (lo, n) in enumerate(((0, 4), (4, GROUP - 4))):
                    pe.wait_ge(hw_scaled, i * 2 + (h + 1))
                    for u in range(n):
                        for c in range(2):
                            last = nc.tensor.matmul(ps[4 + h][:, u * FEAT:(u + 1) * FEAT],
                                                    gT[:, c, (lo + u) * PART:(lo + u + 1) * PART], w2[:, c, :],
                                                    start=(c == 0), stop=(c == 1), skip_group_check=True)
                    last.then_inc(hw_sent, 1)
            multiply_pass(3)

        @block.vector
        def _(v):
            steps = [0]

            def chain(ins):
                steps[0] += 1
                ins.then_inc(dve_chain, 1)
                v.wait_ge(dve_chain, steps[0])

            def rooted(n):
                v.wait_ge(sqrt_done, n)

            nc.vector.memset(xbuf[:, NODE_TILES - 1, :], 0.0).then_inc(x_pad, 1)
            chain(nc.vector.memset(zeros16[:, :], 0.0))
            nc.vector.memset(ones[:, :], 1.0).then_inc(const_ready, 1)
            v.wait_ge(ld_first, 16)
            chain(nc.vector.tensor_single_scalar(dst_first[:, :], dst_first[:, :], SHIFT, ALU.arith_shift_right))
            v.wait_ge(ld_const, 64)
            nc.vector.tensor_tensor(entry[:, :], dst_first[:, :], tile_no[:, :], ALU.add).then_inc(entry_ready, 1)
            nc.vector.tensor_copy(iota16[:, :], iota[:, :]).then_inc(const_ready, 1)
            v.wait_ge(ld_edges, 16)
            chain(nc.vector.tensor_single_scalar(edge_int[:, 0, :, :], edge_rows[:, :, :], PART - 1, ALU.bitwise_and))
            chain(nc.vector.tensor_single_scalar(edge_int[:, 1, :, :], edge_rows[:, :, :], SHIFT, ALU.arith_shift_right))
            nc.vector.tensor_copy(edge_f32[:, :, :, :], edge_int[:, :, :, :]).then_inc(halves_ready, 1)
            v.wait_ge(entry_sent, 1)
            for h in range(2):
                chain(nc.vector.tensor_copy(entry_bc[:, h * (TABLE // 2):(h + 1) * (TABLE // 2)], ps[h][:, 0:TABLE // 2]))
            for k in range(BLOCKS):
                chain(nc.vector.tensor_scalar(between[:, 0:TABLE - 1], entry_bc[:, 1:TABLE],
                                              pair_no[:, k:k + 1], 0.0, ALU.is_le, ALU.add, accum_out=tile_of[:, k:k + 1]))
            chain(nc.vector.tensor_tensor(node_of[:, :], pair_no[:, :], tile_of[:, :], ALU.subtract))
            chain(nc.vector.tensor_single_scalar(node_base[:, :], node_of[:, :], float(PART), ALU.mult))
            v.wait_ge(halves_ready, 1)
            nc.vector.tensor_copy(tile_idx[:, :], tile_of[:, :]).then_inc(pair_tiles_ready, 1)
            v.wait_ge(ld_wa, 96)
            for c in range(2):
                nc.vector.tensor_scalar(b1_rep[:, c, :], ones[:, :], b1_col[:, c:c + 1], None, ALU.mult).then_inc(b1_rep_ready, 1)
            v.wait_ge(ld_x, 16)
            v.wait_ge(ld_x_last, 16)
            chain(nc.vector.tensor_reduce(stat[:, 0, :], xn, AX.X, ALU.add))
            chain(nc.vector.tensor_single_scalar(stat[:, 0, :], stat[:, 0, :], 1.0 / FEAT, ALU.mult))
            nc.vector.tensor_tensor(xn, xn, stat[:, 0, :].unsqueeze(2).to_broadcast([PART, NODE_TILES, FEAT]),
                                    ALU.subtract).then_inc(centred, 1)
            v.wait_ge(node_of_sent, 1)
            nc.vector.tensor_copy(node_rows[:, :], ps[1][0:BLOCKS, 0:PART]).then_inc(node_rows_ready, 1)
            v.wait_ge(const_ready, 2)
            v.wait_ge(setup_moved, 4)
            with v.Fori(0, DEG_TURNS // 2) as i:
                for h in range(2):
                    v.wait_ge(tiles_counted, i * (2 * UNROLL) + (h + 1) * UNROLL)
                    nc.vector.tensor_tensor(
                        high_hot[:, h, :, :],
                        iota16[:, 0:NODE_TILES + 1].unsqueeze(1).to_broadcast([PART, UNROLL, NODE_TILES + 1]),
                        dst_high[:, bass.ds(i * (2 * UNROLL) + h * UNROLL, UNROLL)].unsqueeze(2).to_broadcast(
                            [PART, UNROLL, NODE_TILES + 1]),
                        ALU.is_equal).then_inc(high_ready, 1)
                    for u in range(UNROLL):
                        t = i * (2 * UNROLL) + (h * UNROLL + u)
                        v.wait_ge(tiles_counted, t + (UNROLL + 1))
                        nc.vector.tensor_scalar(low_hot[:, u, :], iota16[:, :], dst_low[:, bass.ds(t, 1)], None,
                                                ALU.is_equal).then_inc(low_ready, 1)
            for k in range(BLOCKS):
                v.wait_ge(got_src[k], 16)
            nc.vector.tensor_copy(edge_f32[:, 0, :, :], edge_int[:, 0, :, :]).then_inc(pair_parts_ready, 1)
            for k in range(BLOCKS):
                v.wait_ge(got_dst[k], 16)
                last = nc.vector.tensor_scalar(edge_f32[:, 1, k, :], edge_int[:, 1, k, :], node_base[:, k:k + 1], None, ALU.subtract)
            last.then_inc(pair_parts_ready, 1)
            v.wait_ge(squared, 1)
            chain(nc.vector.tensor_reduce(stat[:, 1, :], squares, AX.X, ALU.add))
            nc.vector.tensor_scalar(stat[:, 1, :], stat[:, 1, :], 1.0 / FEAT, LN_EPS, ALU.mult, ALU.add).then_inc(sqrt_need, 1)
            v.wait_ge(deg_ready, 1)
            nc.vector.tensor_single_scalar(stat[:, 3, :], ps[2][:, 0:NODE_TILES], 1.0, ALU.add).then_inc(sqrt_need, 1)
            rooted(2)
            chain(nc.vector.reciprocal(stat[:, 2, :], stat[:, 2, :]))
            chain(nc.vector.reciprocal(dinv[:, :], dinv[:, :]))
            chain(nc.vector.tensor_tensor(row_scale[:, :], stat[:, 2, :], dinv[:, :], ALU.mult))

            def by_node(col, i):
                return col[:, GROUP * i:GROUP * (i + 1)].unsqueeze(2).to_broadcast([PART, GROUP, FEAT])

            for i in range(NODE_TURNS):
                t = slice(GROUP * i, GROUP * (i + 1))
                nc.vector.scalar_tensor_tensor(tab1[:, t, :], xn[:, t, :], 0.0, by_node(row_scale, i),
                                               ALU.max, ALU.mult).then_inc(tab_ready, 1)
            nc.vector.memset(acc1[:, SPARE, :], 0.0).then_inc(acc_cleared, 1)
            v.wait_ge(setup_moved, 8 + -(-NODE_TILES // 4))
            nc.vector.memset(acc2, 0.0).then_inc(acc_cleared, 1)
            v.wait_ge(acc_cleared, 2)
            v.wait_ge(ld_node_row, 16)

            def pair_pass(k, acc, cols):
                half = UNROLL // 2
                for h in range(2):
                    nc.vector.tensor_copy(idx_ring[:, h * half:(h + 1) * half],
                                          pair_src[:, h * half:(h + 1) * half]).then_inc(idx_staged, 1)
                with v.Fori(0, TURNS) as i:
                    _, nodes = nc.values_load_multi_w_load_instructions(
                        node_row[0:1, bass.ds(i * UNROLL, UNROLL)], engines=[VEC], min_val=0, max_val=SPARE,
                        skip_runtime_bounds_check_because="the staircase has no more node tiles")

                    def weigh(u):
                        n = i * UNROLL + (PAIRS * k + u)
                        slot, column = weights[:, u % W_RING, :], bass.ds(i * UNROLL + u, 1)
                        v.wait_ge(pairs_done, n + (UNROLL + 1 - W_RING))
                        if k == 3 and u == 0:
                            v.wait_ge(gates_kept, TURNS)
                        if k in (1, 2):
                            v.wait_ge(gates_ready, n + (1 - PAIRS))
                        if k == 0:
                            ins = nc.vector.tensor_scalar(slot, iota[:, :], pair_dst[:, column], None, ALU.is_equal)
                        elif k == 1:
                            ins = nc.vector.scalar_tensor_tensor(slot, iota[:, :], pair_dst[:, column], gates[:, u % W_RING, :],
                                                                 ALU.is_equal, ALU.mult)
                        elif k == 2:
                            ins = nc.vector.scalar_tensor_tensor(slot, iota[:, :], pair_dst[:, column], gates[:, u % W_RING, :],
                                                                 ALU.is_equal, ALU.mult, accum_out=gate_ring[:, u:u + 1])
                        else:
                            ins = nc.vector.tensor_scalar(slot, iota[:, :], pair_dst[:, column], gate2[:, column],
                                                          ALU.is_equal, ALU.mult)
                        ins.then_inc(weights_ready, 1)

                    def add(u):
                        n = i * UNROLL + (PAIRS * k + u)
                        sums = acc[:, bass.ds(nodes[u], 1), 0:cols].rearrange("p o f -> p (o f)")
                        v.wait_ge(pairs_done, n + (UNROLL + 1))
                        v.wait_ge(pairs_added, n + W_RING)
                        nc.vector.tensor_tensor(sums, sums, ps[u % W_RING][:, 0:cols], ALU.add).then_inc(pairs_added, 1)

                    for u in range(UNROLL):
                        weigh(u)
                        if u:
                            add(u - 1)
                        if u == half:
                            v.wait_ge(half_begun, i * 2 + (2 * TURNS * k + 1))
                            nc.vector.tensor_copy(idx_ring[:, 0:half], pair_src[:, bass.ds(i * UNROLL + UNROLL, half)]).then_inc(idx_staged, 1)
                    add(UNROLL - 1)
                    if k == 2:
                        v.wait_ge(weights_ready, i * UNROLL + (PAIRS * k + UNROLL))
                        nc.vector.tensor_copy(gate2[:, bass.ds(i * UNROLL, UNROLL)], gate_ring[:, :]).then_inc(gates_kept, 1)
                        v.wait_ge(gates_kept, i + 1)
                    v.wait_ge(half_begun, i * 2 + (2 * TURNS * k + 2))
                    nc.vector.tensor_copy(idx_ring[:, half:UNROLL], pair_src[:, bass.ds(i * UNROLL + (UNROLL + half), half)]).then_inc(idx_staged, 1)
                v.wait_ge(pairs_added, PAIRS * (k + 1) + W_RING)

            def spread_gates(phase):
                for i in range(NODE_TURNS):
                    if phase or i:
                        v.wait_ge(bc_sent, 2 * (NODE_TURNS * phase + i))
                    nc.vector.tensor_tensor(diag[:, :, :], ident[:, :].unsqueeze(1).to_broadcast([PART, GROUP, PART]),
                                            by_node(gate_dst, i), ALU.mult).then_inc(diag_ready, 1)

            pair_pass(0, acc1, FEAT)
            with v.Fori(0, NODE_TURNS) as i:
                for u in range(GROUP):
                    j = i * GROUP + u
                    v.wait_ge(u_moved, j + (GROUP + 1))
                    v.wait_ge(h_squared, j + 1)
                    nc.vector.scalar_tensor_tensor(hbuf[:, u, :], ps[u][:, 0:HID], dinv[:, bass.ds(j, 1)], b1_bc[:, 0:HID],
                                                   ALU.mult, ALU.add).then_inc(h_ready, 1)
                    nc.vector.scalar_tensor_tensor(att[:, bass.ds(j, 1), :].rearrange("p o f -> p (o f)"), ps[u][:, HID:HID + 2],
                                                   dinv[:, bass.ds(j, 1)], b1_bc[:, HID:HID + 2], ALU.mult, ALU.add).then_inc(psum_read, 1)
            v.wait_ge(psum_read, GROUP + NODE_TILES)
            v.wait_ge(h_squared, GROUP + NODE_TILES)
            nc.vector.memset(tab2[:, :, FEAT + 2:ROW2], 0.0).then_inc(sqrt_need, 1)
            rooted(3)
            chain(nc.vector.tensor_single_scalar(rnorm[:, :], rnorm[:, :], NORM_EPS, ALU.max))
            chain(nc.vector.reciprocal(rnorm[:, :], rnorm[:, :]))
            nc.vector.tensor_copy(tab2[:, :, FEAT], rnorm[:, :])
            nc.vector.tensor_tensor(tab2[:, :, FEAT + 1], att[:, :, 0], rnorm[:, :], ALU.mult)
            chain(nc.vector.tensor_tensor(gate_dst[:, :], att[:, :, 1], rnorm[:, :], ALU.mult))
            chain(nc.vector.tensor_scalar(gate_dst[:, :], gate_dst[:, :], be[:, 0:1], None, ALU.add))
            chain(nc.vector.tensor_tensor(row_scale[:, :], rnorm[:, :], dinv[:, :], ALU.mult))
            v.wait_ge(u_moved, GROUP + NODE_TILES)
            for i in range(NODE_TURNS):
                t = slice(GROUP * i, GROUP * (i + 1))
                nc.vector.tensor_tensor(tab2[:, t, 0:FEAT], tab2[:, t, 0:FEAT], by_node(row_scale, i), ALU.mult).then_inc(tab_ready, 1)
            chain(nc.vector.memset(xbuf[:, SPARE, :], 0.0))
            spread_gates(0)
            pair_pass(1, acc2, FEAT + 1)
            v.wait_ge(tab_stored[1], 16 * NODE_TURNS)
            nc.vector.memset(tab3[:, :, HID + 1:ROW3], 0.0)
            with v.Fori(0, NODE_TURNS) as i:
                def score(u):
                    v.wait_ge(act3_ready, i * GROUP + (u + 1))
                    if u:
                        v.wait_ge(scored, i * (2 * GROUP) + 2 * u)
                    for c in range(2):
                        nc.vector.tensor_tensor_reduce(scrap[:, c, :], hbuf[:, u, :], we2_bc[:, c, :], 1.0, 0.0, ALU.mult, ALU.add,
                                                       scores[:, u, c:c + 1]).then_inc(scored, 1)

                for u in range(GROUP):
                    j = i * GROUP + u
                    v.wait_ge(tiles_done, j + (NODE_TILES + GROUP + 1))
                    v.wait_ge(rows3_ready, j + 1)
                    nc.vector.scalar_tensor_tensor(hbuf[:, u, :], b1n_bc[:, :], acc2[:, bass.ds(j, 1), FEAT], ps[u][:, 0:HID],
                                                   ALU.mult, ALU.add).then_inc(pre_ready, 1)
                    if u:
                        score(u - 1)
                score(GROUP - 1)
                v.wait_ge(scored, i * (2 * GROUP) + 2 * GROUP)
                nc.vector.tensor_copy(gate_dst[:, bass.ds(i * GROUP, GROUP)], scores[:, :, 1])
                v.wait_ge(rows3_ready, i * GROUP + 2 * GROUP)
                nc.vector.tensor_copy(tab3[:, bass.ds(i * GROUP, GROUP), HID], scores[:, :, 0]).then_inc(tab_ready, 1)
            v.wait_ge(tab_ready, 3 * NODE_TURNS)
            chain(nc.vector.tensor_scalar(gate_dst[:, :], gate_dst[:, :], be[:, 1:2], None, ALU.add))
            spread_gates(1)
            chain(nc.vector.memset(acc3, 0.0))
            pair_pass(2, acc3, HID + 1)
            nc.vector.tensor_single_scalar(stat[:, 0, :], acc3[:, 0:NODE_TILES, HID], 1.0, ALU.add).then_inc(sqrt_need, 1)
            rooted(4)
            chain(nc.vector.reciprocal(dinv2[:, :], dinv2[:, :]))
            v.wait_ge(tab_stored[2], 16 * NODE_TURNS)
            with v.Fori(0, NODE_TURNS) as i:
                for h, (lo, n) in enumerate(((0, 4), (4, GROUP - 4))):
                    v.wait_ge(hw_sent, i * 2 + (h + 3))
                    ins = nc.vector.tensor_tensor(
                        tab4[:, bass.ds(i * GROUP + lo, n), :], ps[4 + h][:, 0:n * FEAT].rearrange("p (j f) -> p j f", f=FEAT),
                        dinv2[:, bass.ds(i * GROUP + lo, n)].unsqueeze(2).to_broadcast([PART, n, FEAT]), ALU.mult)
                    ins.then_inc(hw_scaled, 1)
                v.wait_ge(hw_scaled, i * 2 + 4)
                nc.vector.tensor_copy(scores[:, 0, :], be[:, :]).then_inc(tab_ready, 1)
            chain(nc.vector.memset(acc4[:, SPARE, :], 0.0))
            v.wait_ge(ld_x2, 32)
            chain(nc.vector.tensor_tensor(xn, xn, b2_bc[:, :].unsqueeze(1).to_broadcast([PART, NODE_TILES, FEAT]), ALU.add))
            v.wait_ge(tab_stored[3], 16 * NODE_TURNS)
            pair_pass(3, acc4, FEAT)
            for i in range(NODE_TURNS):
                t = slice(GROUP * i, GROUP * (i + 1))
                chain(nc.vector.tensor_tensor(acc4[:, t, :], acc4[:, t, :], by_node(dinv2, i), ALU.mult))
                nc.vector.tensor_tensor(acc4[:, t, :], acc4[:, t, :], xn[:, t, :], ALU.add).then_inc(fin_ready, 1)


def kernel(x, src, dst, L0_gnn_W1, L0_gnn_b1, L0_gnn_We1, L0_gnn_be1, L0_gnn_Wn1, L0_gnn_bn1,
           L0_gnn_We2, L0_gnn_be2, L0_gnn_W2, L0_gnn_b2):
    import numpy as np
    import concourse.bacc as bacc
    from concourse import mybir as mb
    from concourse.bass_utils import run_bass_kernel_spmd

    def edge_tiles(e, pad):
        e = np.asarray(e)
        full = np.full(TABLE * PART, pad, e.dtype)
        full[:EDGES] = e
        return full.reshape(TABLE, PART)

    arrays = {
        "x": x, "src": edge_tiles(src, 0), "dst": edge_tiles(dst, PAD_DST),
        "W1": L0_gnn_W1, "b1": L0_gnn_b1, "We1": L0_gnn_We1, "be1": L0_gnn_be1, "Wn1": L0_gnn_Wn1,
        "bn1": L0_gnn_bn1, "We2": L0_gnn_We2, "be2": L0_gnn_be2, "W2": L0_gnn_W2, "b2": L0_gnn_b2,
        "ident": np.eye(PART, dtype=np.float32),
        "iota": np.tile(np.arange(PART, dtype=np.float32), (PART, 1)),
        "pair_no": np.arange(TABLE, dtype=np.float32).reshape(BLOCKS, PART).T,
        "tile_no": np.arange(TABLE, dtype=np.float32).reshape(1, TABLE),
    }
    nc = bacc.Bacc("TRN2", target_bir_lowering=False, num_devices=1)
    given, args = {}, []
    for name, a in arrays.items():
        a = np.ascontiguousarray(a)
        given[f"in_{name}"] = a
        args.append(nc.dram_tensor(f"in_{name}", a.shape, mb.dt.from_np(a.dtype), kind="ExternalInput").ap())
    result = nc.dram_tensor("out_nodes", (NODES, FEAT), mb.dt.float32, kind="ExternalOutput").ap()
    gnn_kernel(nc, *args, result)
    return run_bass_kernel_spmd(nc, [given], core_ids=[0]).results[0]["out_nodes"]
```
